# Optimizing a Trainium2 kernel written in Bass

```python
import numpy as np
import jax
import jax.numpy as jnp

def _softmax(x, axis=-1):
    return jax.nn.softmax(x, axis=axis)

def _gelu(x):
    return jax.nn.gelu(x, approximate=True)

def _silu(x):
    return jax.nn.silu(x)

def _sigmoid(x):
    return jax.nn.sigmoid(x)

def _layernorm(x, axis=-1, eps=1e-05):
    m = jnp.mean(x, axis=axis, keepdims=True)
    v = jnp.var(x, axis=axis, keepdims=True)
    return (x - m) / jnp.sqrt(v + eps)

def _scatter_add(tgt, idx, src, axis=0):
    return tgt.at[idx].add(src)

def _segment_sum(src, seg, n):
    return jax.ops.segment_sum(src, seg, n)
kernel_name = 'mk_dlrm_tower_d1_rec_r8_c0b0ef'

def setup_inputs(seed: int=0):
    np.random.seed(seed)
    _w = jnp.asarray

    def _rec_inputs():
        import jax
        import jax.numpy as jnp
        _tk = jax.random.key(seed)
        ids = jnp.stack([jax.random.randint(jax.random.fold_in(_tk, 200 + f), (512,), 0, v, jnp.int32) for f, v in enumerate([1000, 1000, 12500, 1250, 12500, 125000, 1250, 1000, 12500, 12500, 1000, 12500, 12500, 12500, 1250, 1250, 12500, 12500, 1000, 1000, 1000, 1000, 1000, 1000, 1000, 1000])], axis=1)
        tbl_0 = 0.05 * jax.random.normal(jax.random.fold_in(_tk, 500 + 0), (1000, 128), jnp.float32)
        tbl_1 = 0.05 * jax.random.normal(jax.random.fold_in(_tk, 500 + 1), (1000, 128), jnp.float32)
        tbl_2 = 0.05 * jax.random.normal(jax.random.fold_in(_tk, 500 + 2), (12500, 128), jnp.float32)
        tbl_3 = 0.05 * jax.random.normal(jax.random.fold_in(_tk, 500 + 3), (1250, 128), jnp.float32)
        tbl_4 = 0.05 * jax.random.normal(jax.random.fold_in(_tk, 500 + 4), (12500, 128), jnp.float32)
        tbl_5 = 0.05 * jax.random.normal(jax.random.fold_in(_tk, 500 + 5), (125000, 128), jnp.float32)
        tbl_6 = 0.05 * jax.random.normal(jax.random.fold_in(_tk, 500 + 6), (1250, 128), jnp.float32)
        tbl_7 = 0.05 * jax.random.normal(jax.random.fold_in(_tk, 500 + 7), (1000, 128), jnp.float32)
        tbl_8 = 0.05 * jax.random.normal(jax.random.fold_in(_tk, 500 + 8), (12500, 128), jnp.float32)
        tbl_9 = 0.05 * jax.random.normal(jax.random.fold_in(_tk, 500 + 9), (12500, 128), jnp.float32)
        tbl_10 = 0.05 * jax.random.normal(jax.random.fold_in(_tk, 500 + 10), (1000, 128), jnp.float32)
        tbl_11 = 0.05 * jax.random.normal(jax.random.fold_in(_tk, 500 + 11), (12500, 128), jnp.float32)
        tbl_12 = 0.05 * jax.random.normal(jax.random.fold_in(_tk, 500 + 12), (12500, 128), jnp.float32)
        tbl_13 = 0.05 * jax.random.normal(jax.random.fold_in(_tk, 500 + 13), (12500, 128), jnp.float32)
        tbl_14 = 0.05 * jax.random.normal(jax.random.fold_in(_tk, 500 + 14), (1250, 128), jnp.float32)
        tbl_15 = 0.05 * jax.random.normal(jax.random.fold_in(_tk, 500 + 15), (1250, 128), jnp.float32)
        tbl_16 = 0.05 * jax.random.normal(jax.random.fold_in(_tk, 500 + 16), (12500, 128), jnp.float32)
        tbl_17 = 0.05 * jax.random.normal(jax.random.fold_in(_tk, 500 + 17), (12500, 128), jnp.float32)
        tbl_18 = 0.05 * jax.random.normal(jax.random.fold_in(_tk, 500 + 18), (1000, 128), jnp.float32)
        tbl_19 = 0.05 * jax.random.normal(jax.random.fold_in(_tk, 500 + 19), (1000, 128), jnp.float32)
        tbl_20 = 0.05 * jax.random.normal(jax.random.fold_in(_tk, 500 + 20), (1000, 128), jnp.float32)
        tbl_21 = 0.05 * jax.random.normal(jax.random.fold_in(_tk, 500 + 21), (1000, 128), jnp.float32)
        tbl_22 = 0.05 * jax.random.normal(jax.random.fold_in(_tk, 500 + 22), (1000, 128), jnp.float32)
        tbl_23 = 0.05 * jax.random.normal(jax.random.fold_in(_tk, 500 + 23), (1000, 128), jnp.float32)
        tbl_24 = 0.05 * jax.random.normal(jax.random.fold_in(_tk, 500 + 24), (1000, 128), jnp.float32)
        tbl_25 = 0.05 * jax.random.normal(jax.random.fold_in(_tk, 500 + 25), (1000, 128), jnp.float32)
        _rk = jax.random.fold_in(_tk, 7)
        r_dense_proj = -0.000520686 + 1.00062 * jax.random.normal(jax.random.fold_in(_rk, 101), (512, 128), jnp.float32)
        W_top1 = 0.0405887 * jax.random.normal(jax.random.fold_in(_tk, 801), (607, 512), jnp.float32)
        W_top2 = 0.0441942 * jax.random.normal(jax.random.fold_in(_tk, 802), (512, 256), jnp.float32)
        W_top3 = 0.0625 * jax.random.normal(jax.random.fold_in(_tk, 803), (256, 1), jnp.float32)
        b_top1 = jnp.zeros((512,), jnp.float32)
        b_top2 = jnp.zeros((256,), jnp.float32)
        return (r_dense_proj, ids, tbl_0, tbl_1, tbl_2, tbl_3, tbl_4, tbl_5, tbl_6, tbl_7, tbl_8, tbl_9, tbl_10, tbl_11, tbl_12, tbl_13, tbl_14, tbl_15, tbl_16, tbl_17, tbl_18, tbl_19, tbl_20, tbl_21, tbl_22, tbl_23, tbl_24, tbl_25, W_top1, b_top1, W_top2, b_top2, W_top3)
    r_dense_proj, ids, tbl_0, tbl_1, tbl_2, tbl_3, tbl_4, tbl_5, tbl_6, tbl_7, tbl_8, tbl_9, tbl_10, tbl_11, tbl_12, tbl_13, tbl_14, tbl_15, tbl_16, tbl_17, tbl_18, tbl_19, tbl_20, tbl_21, tbl_22, tbl_23, tbl_24, tbl_25, W_top1, b_top1, W_top2, b_top2, W_top3 = _rec_inputs()

    def _L0_rec_setup():
        import jax, jax.numpy as jnp
        import numpy as np
        key = jax.random.key(seed)
        k1, k2 = jax.random.split(key)
        B, N_SPARSE, D = (2048, 26, 128)
        dense_proj = jax.random.normal(k1, (B, D), dtype=jnp.float32)
        sparse_embs = jax.random.normal(k2, (B, N_SPARSE, D), dtype=jnp.float32)
        return {'dense_proj': dense_proj, 'sparse_embs': sparse_embs}
    _L0_rec_all = _L0_rec_setup()
    _L0_rec_in = {k: v for k, v in _L0_rec_all.items() if k in ()}
    del _L0_rec_all
    return {'r_dense_proj': r_dense_proj, 'ids': ids, 'tbl_0': tbl_0, 'tbl_1': tbl_1, 'tbl_2': tbl_2, 'tbl_3': tbl_3, 'tbl_4': tbl_4, 'tbl_5': tbl_5, 'tbl_6': tbl_6, 'tbl_7': tbl_7, 'tbl_8': tbl_8, 'tbl_9': tbl_9, 'tbl_10': tbl_10, 'tbl_11': tbl_11, 'tbl_12': tbl_12, 'tbl_13': tbl_13, 'tbl_14': tbl_14, 'tbl_15': tbl_15, 'tbl_16': tbl_16, 'tbl_17': tbl_17, 'tbl_18': tbl_18, 'tbl_19': tbl_19, 'tbl_20': tbl_20, 'tbl_21': tbl_21, 'tbl_22': tbl_22, 'tbl_23': tbl_23, 'tbl_24': tbl_24, 'tbl_25': tbl_25, 'W_top1': W_top1, 'b_top1': b_top1, 'W_top2': W_top2, 'b_top2': b_top2, 'W_top3': W_top3}

def reference(r_dense_proj, ids, tbl_0, tbl_1, tbl_2, tbl_3, tbl_4, tbl_5, tbl_6, tbl_7, tbl_8, tbl_9, tbl_10, tbl_11, tbl_12, tbl_13, tbl_14, tbl_15, tbl_16, tbl_17, tbl_18, tbl_19, tbl_20, tbl_21, tbl_22, tbl_23, tbl_24, tbl_25, W_top1, b_top1, W_top2, b_top2, W_top3):
    import jax
    import jax.numpy as jnp

    def _L0_rec_ref(dense_proj, sparse_embs):
        import jax, jax.numpy as jnp
        import numpy as np
        all_vecs = jnp.concatenate([dense_proj[:, None, :], sparse_embs], axis=1)
        n = all_vecs.shape[1]
        interactions = jnp.einsum('bnd,bmd->bnm', all_vecs, all_vecs)
        rows, cols = np.triu_indices(n, k=1)
        interact_flat = interactions[:, rows, cols]
        return jnp.concatenate([dense_proj, interact_flat], axis=1)
    e = jnp.stack([tbl_0[ids[:, 0]], tbl_1[ids[:, 1]], tbl_2[ids[:, 2]], tbl_3[ids[:, 3]], tbl_4[ids[:, 4]], tbl_5[ids[:, 5]], tbl_6[ids[:, 6]], tbl_7[ids[:, 7]], tbl_8[ids[:, 8]], tbl_9[ids[:, 9]], tbl_10[ids[:, 10]], tbl_11[ids[:, 11]], tbl_12[ids[:, 12]], tbl_13[ids[:, 13]], tbl_14[ids[:, 14]], tbl_15[ids[:, 15]], tbl_16[ids[:, 16]], tbl_17[ids[:, 17]], tbl_18[ids[:, 18]], tbl_19[ids[:, 19]], tbl_20[ids[:, 20]], tbl_21[ids[:, 21]], tbl_22[ids[:, 22]], tbl_23[ids[:, 23]], tbl_24[ids[:, 24]], tbl_25[ids[:, 25]]], axis=1)
    z = _L0_rec_ref(r_dense_proj, e)
    z = z.reshape(z.shape[0], -1)
    h = jnp.concatenate([z, r_dense_proj], axis=1)
    h = jnp.maximum(h @ W_top1 + b_top1, 0.0)
    h = jnp.maximum(h @ W_top2 + b_top2, 0.0)
    y = h @ W_top3
    return y

_drawn_inputs = setup_inputs


def setup_inputs(seed=0):
    import zlib

    import numpy as np

    out = dict(_drawn_inputs(seed))
    spreads = {'b_top1': (0.0, 0.1), 'b_top2': (0.0, 0.1)}
    factors = {}
    for name, (base, spread) in spreads.items():
        noise = np.random.default_rng([zlib.crc32(name.encode()), seed]).standard_normal(out[name].shape)
        drawn = base * np.exp(spread * noise) if base else spread * noise
        out[name] = jnp.asarray(drawn.astype(out[name].dtype))
    for name, factor in factors.items():
        out[name] = (out[name] * factor).astype(out[name].dtype)
    return out
```

```python
import concourse.bass as bass
from concourse import mybir
from contextlib import ExitStack

P = 128
BATCH, D = 512, 128
NTAB = 26
NVEC = NTAB + 1
SLOTS = 32
H1, H2 = 512, 256
TILES = BATCH // P
QUADS = 4
NCOL = NVEC - 1
GROUPS = P // QUADS
GB = 8
NGB = GROUPS // GB
TURNS = [range(4 * q, min(4 * q + 4, NVEC)) for q in range((NVEC + 3) // 4)]
NTURN = len(TURNS)
MH = (NCOL + 3) // 4
ONES_ROW = 96
KT = MH + 2
F32 = mybir.dt.float32
I32 = mybir.dt.int32
ALU = mybir.AluOpType
ACT = mybir.ActivationFunctionType


def pulls(quads):
    return [(j, mq, len(range(mq, NCOL, 4))) for j in quads for mq in range(4)]


def dlrm_tower(nc, dense, ids, tables, w1, w2, b2, w3, out):
    ctx = ExitStack()
    with ctx:
        def sb(name, shape, dtype=F32):
            return ctx.enter_context(nc.sbuf_tensor(name, shape, dtype))

        def pb(name, shape):
            return ctx.enter_context(nc.psum_tensor(name, shape, F32))

        def sem(name):
            return ctx.enter_context(nc.semaphore(name))

        idx = sb("idx", [P, TILES, NTAB], I32)
        ident = sb("ident", [P, P])
        vecs = sb("vecs", [P, NVEC, D])
        XT = sb("XT", [P, P, SLOTS])
        Z = sb("Z", [P, MH, P])
        w1_sb = sb("w1_sb", [P, KT, H1])
        w2_sb = sb("w2_sb", [P, H1 // P, H2])
        b2_sb = sb("b2_sb", [P, H2])
        w3_sb = sb("w3_sb", [P, H2])
        h1 = sb("h1", [P, H1])
        h1T = sb("h1T", [P, H1 // P, P])
        h2 = sb("h2", [P, H2])
        h2r = sb("h2r", [P, H2])
        y = sb("y", [P, 1])

        turn_ps = [pb(f"turn_ps{i}", [P, 4, P]) for i in range(2)]
        gram_ps = [pb(f"gram_ps{i}", [P, GB, P]) for i in range(2)]
        h1_ps = pb("h1_ps", [P, H1])
        h2_ps = pb("h2_ps", [P, 2 * H2])

        ids_in = sem("ids_in")
        dense_in = sem("dense_in")
        w1_in = sem("w1_in")
        w2_in = sem("w2_in")
        rows_in = sem("rows_in")
        gathered = [sem(f"gathered{q}") for q in range(NTURN)]
        ident_zero = sem("ident_zero")
        ident_set = sem("ident_set")
        pads_set = sem("pads_set")
        w1_added = sem("w1_added")
        turned = sem("turned")
        xt_by_dve = sem("xt_by_dve")
        xt_by_act = sem("xt_by_act")
        grams = sem("grams")
        pulled_dve = sem("pulled_dve")
        pulled_act = sem("pulled_act")
        h1_summed = sem("h1_summed")
        h1_ready = sem("h1_ready")
        h2_summed = sem("h2_summed")
        h2_biased = sem("h2_biased")
        h2_relued = sem("h2_relued")
        y_ready = sem("y_ready")
        y_stored = sem("y_stored")

        block = ctx.enter_context(nc.Block())

        @block.sync
        def _(sp):
            sp.dma_start(idx[:], ids).then_inc(ids_in, 16)

            def tile(t, first):
                if not first:
                    sp.wait_ge(turned, (NTURN + 1) * (t - 1) + 1)
                sp.dma_start(vecs[:, 0, :], dense[bass.ds(t * P, P), :]).then_inc(dense_in, 16)
                if first:
                    sp.dma_start(w1_sb[:], w1).then_inc(w1_in, 16)
                    sp.dma_start(w2_sb[:], w2).then_inc(w2_in, 16)
                    sp.dma_start(b2_sb[:], b2.partition_broadcast(P)).then_inc(rows_in, 16)
                    sp.dma_start(w3_sb[:], w3.partition_broadcast(P)).then_inc(rows_in, 16)
                else:
                    store(t - 1)

            def store(t):
                sp.wait_ge(y_ready, t + 1)
                sp.dma_start(out[bass.ds(t * P, P), :], y[:]).then_inc(y_stored, 16)

            tile(0, True)
            with sp.Fori(1, TILES) as t:
                tile(t, False)
            store(TILES - 1)
            sp.wait_ge(y_stored, 16 * TILES)

        @block.gpsimd
        def _(pool):
            pool.memset(ident[:], 0.0).then_inc(ident_zero, 1)
            pool.wait_ge(ident_zero, 1)
            pool.affine_select(out=ident[:], in_=ident[:], compare_op=ALU.not_equal, fill=1.0,
                               base=0, pattern=[[-1, P]], channel_multiplier=1).then_inc(ident_set, 1)
            pool.wait_ge(ids_in, 16)
            for t in range(TILES):
                for q, slots in enumerate(TURNS):
                    if t >= 1:
                        pool.wait_ge(turned, (NTURN + 1) * (t - 1) + q + 1)
                    for slot in slots:
                        if slot >= 1:
                            f = slot - 1
                            pool.indirect_dma_start(
                                vecs[:, slot, :], None, tables[f],
                                bass.IndirectOffsetOnAxis(ap=idx[:, t, f:f + 1], axis=0),
                            ).then_inc(gathered[q], 16)

        def copy_turned(eng, copy, q, t, done):
            slots = TURNS[q]
            eng.wait_ge(turned, (NTURN + 1) * t + q + 1)
            copy(XT[:, :, slots[0]:slots[-1] + 1],
                 turn_ps[q % 2][:, 0:len(slots), :].rearrange("p f b -> p b f")).then_inc(done, 1)

        def pull(eng, copy, quads, t, done):
            for k in range(NGB):
                eng.wait_ge(grams, NGB * t + k + 1)
                for j, mq, n in pulls(quads):
                    last = copy(
                        Z[32 * mq:32 * mq + 32, 0:n, 4 * GB * k + j:4 * GB * (k + 1):4].rearrange("p m g -> p g m"),
                        gram_ps[k % 2][32 * j:32 * j + 32, :, NCOL * j + mq:NCOL * (j + 1):4])
                last.then_inc(done, 1)

        @block.vector
        def _(dve):
            dve.memset(XT[:, :, NVEC:SLOTS], 0.0).then_inc(pads_set, 1)
            dve.memset(Z[64:128, MH - 1, :], 0.0).then_inc(pads_set, 1)
            dve.wait_ge(pads_set, 2)
            dve.memset(Z[ONES_ROW:ONES_ROW + 1, MH - 1, :], 1.0).then_inc(pads_set, 1)
            dve.wait_ge(w1_in, 16)
            dve.tensor_tensor(w1_sb[:, MH, :], w1_sb[:, MH, :], w1_sb[:, MH + 1, :], ALU.add).then_inc(w1_added, 1)
            dve.wait_ge(rows_in, 32)

            def tile(t, first):
                for q in range(0, NTURN, 2):
                    copy_turned(dve, nc.vector.tensor_copy, q, t, xt_by_dve)
                pull(dve, nc.vector.tensor_copy, (0, 1), t, pulled_dve)
                dve.wait_ge(h2_summed, t + 1)
                dve.tensor_tensor(h2[:], h2_ps[:, 0:H2], b2_sb[:], ALU.add).then_inc(h2_biased, 1)
                dve.wait_ge(h2_biased, t + 1)
                dve.tensor_scalar(h2r[:], h2[:], 0.0, None, ALU.max).then_inc(h2_relued, 1)
                dve.wait_ge(h2_relued, t + 1)
                if not first:
                    dve.wait_ge(y_stored, 16 * t)
                dve.tensor_tensor_reduce(h2[:], h2r[:], w3_sb[:], 1.0, 0.0, ALU.mult, ALU.add,
                                         y[:, 0:1]).then_inc(y_ready, 1)

            tile(0, True)
            with dve.Fori(1, TILES) as t:
                tile(t, False)

        @block.scalar
        def _(act):
            def copy(o, i):
                return nc.scalar.activation(o, i, ACT.Copy)

            act.wait_ge(pads_set, 3)

            def tile(t):
                for q in range(1, NTURN, 2):
                    copy_turned(act, copy, q, t, xt_by_act)
                pull(act, copy, (2, 3), t, pulled_act)
                act.wait_ge(h1_summed, t + 1)
                nc.scalar.activation(h1[:], h1_ps[:], ACT.Relu).then_inc(h1_ready, 1)
                act.wait_ge(turned, (NTURN + 1) * (t + 1))
                copy(h1T[:], turn_ps[1][:]).then_inc(xt_by_act, 1)

            tile(0)
            with act.Fori(1, TILES) as t:
                tile(t)

        @block.tensor
        def _(pe):
            pe.wait_ge(ident_set, 1)

            def tile(t, first):
                for q, slots in enumerate(TURNS):
                    if q == 0:
                        pe.wait_ge(dense_in, 16 * (t + 1))
                    pe.wait_ge(gathered[q], 16 * len([s for s in slots if s >= 1]) * (t + 1))
                    if not (first and q < 2):
                        pe.wait_ge((xt_by_dve, xt_by_act)[q % 2], 4 * t + q // 2)
                    for i, slot in enumerate(slots):
                        mm = nc.tensor.transpose(turn_ps[q % 2][:, i, :], vecs[:, slot, :], ident[:])
                    mm.then_inc(turned, 1)
                pe.wait_ge(xt_by_dve, 4 * t + 4)
                pe.wait_ge(xt_by_act, 4 * t + 3)
                if first:
                    pe.wait_ge(pads_set, 3)
                for k in range(NGB):
                    if not (first and k < 2):
                        pe.wait_ge(pulled_dve, NGB * t + k - 1)
                        pe.wait_ge(pulled_act, NGB * t + k - 1)
                    for g in range(GB):
                        b = QUADS * (GB * k + g)
                        mm = nc.tensor.matmul(gram_ps[k % 2][:, g, 0:QUADS * NCOL],
                                              XT[:, b:b + QUADS, :].rearrange("p b s -> p (b s)"),
                                              XT[:, b:b + QUADS, 1:NVEC], start=True, stop=True)
                    mm.then_inc(grams, 1)
                if first:
                    pe.wait_ge(w1_added, 1)
                else:
                    pe.wait_ge(h1_ready, t)
                nc.tensor.matmul(h1_ps[:], XT[:, :, 0], w1_sb[:, MH, :], start=True, stop=False)
                pe.wait_ge(pulled_dve, NGB * (t + 1))
                pe.wait_ge(pulled_act, NGB * (t + 1))
                for mh in range(MH):
                    mm = nc.tensor.matmul(h1_ps[:], Z[:, mh, :], w1_sb[:, mh, :], start=False, stop=mh == MH - 1)
                mm.then_inc(h1_summed, 1)
                pe.wait_ge(h1_ready, t + 1)
                pe.wait_ge(xt_by_act, 4 * t + 3)
                for c in range(H1 // P):
                    mm = nc.tensor.transpose(turn_ps[1][:, c, :], h1[:, c * P:(c + 1) * P], ident[:])
                mm.then_inc(turned, 1)
                if first:
                    pe.wait_ge(w2_in, 16)
                else:
                    pe.wait_ge(h2_biased, t)
                pe.wait_ge(xt_by_act, 4 * t + 4)
                for c in range(H1 // P):
                    mm = nc.tensor.matmul(h2_ps[:, 0:H2], h1T[:, c, :], w2_sb[:, c, :],
                                          start=c == 0, stop=c == H1 // P - 1)
                mm.then_inc(h2_summed, 1)

            tile(0, True)
            with pe.Fori(1, TILES) as t:
                tile(t, False)


def w1_rows():
    import numpy as np
    pairs = NVEC * (NVEC - 1) // 2
    bias, zero = D + pairs + D, D + pairs + D + 1
    rows = np.full((P, KT), zero)
    for n in range(NVEC):
        for m in range(n + 1, NVEC):
            mh, mq = divmod(m - 1, 4)
            rows[32 * mq + n, mh] = D + n * (2 * NVEC - n - 1) // 2 + m - n - 1
    rows[ONES_ROW, MH - 1] = bias
    rows[:, MH] = np.arange(D)
    rows[:, MH + 1] = D + pairs + np.arange(D)
    return rows


def kernel(**inputs):
    import numpy as np
    import concourse.bacc as bacc
    from concourse.bass_utils import run_bass_kernel_spmd as run

    w1 = np.concatenate([inputs["W_top1"], np.asarray(inputs["b_top1"])[None, :],
                         np.zeros((1, H1), np.float32)])[w1_rows()]
    arrays = {
        "dense": inputs["r_dense_proj"],
        "ids": np.asarray(inputs["ids"]).reshape(TILES, P, NTAB).transpose(1, 0, 2),
        "w1": w1,
        "w2": np.asarray(inputs["W_top2"]).reshape(H1 // P, P, H2).transpose(1, 0, 2),
        "b2": inputs["b_top2"],
        "w3": np.asarray(inputs["W_top3"])[:, 0],
    }
    arrays |= {f"tbl_{i}": inputs[f"tbl_{i}"] for i in range(NTAB)}
    arrays = {k: np.ascontiguousarray(v) for k, v in arrays.items()}

    nc = bacc.Bacc("TRN2", target_bir_lowering=False, num_devices=1)
    ap = {k: nc.dram_tensor(k, v.shape, mybir.dt.from_np(v.dtype), kind="ExternalInput").ap()
          for k, v in arrays.items()}
    out = nc.dram_tensor("y_out", (BATCH, 1), F32, kind="ExternalOutput").ap()
    dlrm_tower(nc, ap["dense"], ap["ids"], [ap[f"tbl_{i}"] for i in range(NTAB)],
               ap["w1"], ap["w2"], ap["b2"], ap["w3"], out)
    return run(nc, [arrays], core_ids=[0]).results[0]["y_out"]
```

```python
import concourse.bass as bass
from concourse import mybir
from contextlib import ExitStack

P = 128
BATCH, D = 512, 128
NTAB = 26
NVEC = NTAB + 1
SLOTS = 32
H1, H2 = 512, 256
TILES = BATCH // P
QUADS = 4
NCOL = NVEC - 1
GROUPS = P // QUADS
GB = 8
NGB = GROUPS // GB
MH = (NCOL + 3) // 4
ONES_ROW = 96
ZT = MH + 1
W1P = (ZT + 2) // 2
CH = 8
ONEHOT = [(0, 0), (1, 0), (7, 0), (10, 0), (18, 1)]
F32 = mybir.dt.float32
F32R = mybir.dt.float32r
I32 = mybir.dt.int32
ALU = mybir.AluOpType
ACT = mybir.ActivationFunctionType

_HOT = [f for f, _ in ONEHOT]
SLOT_VEC = [0] + [1 + f for f in range(NTAB) if f not in _HOT] + [1 + f for f in reversed(_HOT)]
SLOT_OF = {v - 1: s for s, v in enumerate(SLOT_VEC) if v}


def turns(t):
    n = NVEC - sum(t >= first for _, first in ONEHOT)
    return [range(b, min(b + 4, n)) for b in range(0, n, 4)]


def program():
    always = [i for i, (_, first) in enumerate(ONEHOT) if first == 0]
    later = [i for i, (_, first) in enumerate(ONEHOT) if first > 0]
    rows = {t: [("rows", t, b) for b in range(len(turns(t)))] for t in range(TILES)}
    steps = [("split", 0), ("split", 1)]
    for i in always:
        if i == always[-1]:
            steps += [("w1", 0), ("w1", 1)]
        steps += [("onehot", i)] + [("split", i + 2)] * (i + 2 in always) + rows[0][:1]
        del rows[0][:1]
    steps += rows[0]
    for t in range(TILES):
        after = rows.get(t + 1, []) + 6 * [None]
        steps += [("hidden", t - 1)] * (t > 0) + [("gram", t, 0), after[0]]
        steps += [("w1", 2)] * (t == 0)
        steps += [("second", t - 1)] * (t > 0) + [("gram", t, 1), after[1]]
        steps += [("w1", 3)] * (t == 0)
        steps += [("gram", t, 2)]
        steps += [("w1", 4)] * (t == 0)
        steps += [("gram", t, 3), after[2]]
        steps += [("first", t)] + [("split", i) for i in later if t == 0] + [("relu", t)]
        steps += [("onehot", i) for i in later if t == 0] + after[3:]
    last_rows = ("rows", TILES - 1, len(turns(TILES - 1)) - 1)
    for step in (("hidden", TILES - 2), ("second", TILES - 2)):
        steps.remove(step)
        steps.insert(steps.index(last_rows), step)
    return [s for s in steps if s] + [("hidden", TILES - 1), ("second", TILES - 1)]


PROGRAM = program()
EVENTS = [s for s in PROGRAM if s[0] in ("onehot", "rows", "hidden")]
FIRST_GRAM = EVENTS.index([s for s in PROGRAM[:PROGRAM.index(("gram", 0, 0))] if s in EVENTS][-1]) + 1
EMPTIER = ["act" if n < FIRST_GRAM or n % 2 else "dve" for n in range(len(EVENTS))]


def emptied(n):
    return EMPTIER[n], EMPTIER[:n + 1].count(EMPTIER[n])


def fills(t):
    return [n for n, s in enumerate(EVENTS)
            if s[0] == "rows" and s[1] == t or s[0] == "onehot" and ONEHOT[s[1]][1] <= t]


def pulls(quads):
    return [(j, mq, len(range(mq, NCOL, 4))) for j in quads for mq in range(4)]


def dlrm_tower(nc, dense, ids, hot_ids, hot_tables, tables, w1, w2, b2, w3, out):
    ctx = ExitStack()
    with ctx:
        def sb(name, shape, dtype=F32):
            return ctx.enter_context(nc.sbuf_tensor(name, shape, dtype))

        def pb(name, shape):
            return ctx.enter_context(nc.psum_tensor(name, shape, F32))

        def sem(name):
            return ctx.enter_context(nc.semaphore(name))

        idx = sb("idx", [P, TILES, NTAB], I32)
        ident = sb("ident", [P, P])
        vecs = sb("vecs", [P, 2, len(turns(0)) * 4, D])
        XT = sb("XT", [P, TILES, P, SLOTS])
        Z = sb("Z", [P, MH, P])
        Zh = sb("Zh", [P, ZT, P], F32R)
        Zl = sb("Zl", [P, ZT, P], F32R)
        row_i = sb("row_i", [P, CH], I32)
        row = sb("row", [P, CH])
        hot_id = sb("hot_id", [P, 2, BATCH], I32)
        raw = sb("raw", [P, 2, CH, D])
        high = sb("high", [P, 2, CH, D], F32R)
        low = sb("low", [P, 2, CH, D], F32R)
        hot = sb("hot", [P, CH, BATCH], F32R)
        w1_raw = sb("w1_raw", [P, 2, 2, H1])
        w1h = sb("w1h", [P, ZT, H1], F32R)
        w1l = sb("w1l", [P, ZT, H1], F32R)
        w2_sb = sb("w2_sb", [P, H1 // P, H2])
        b2_sb = sb("b2_sb", [P, H2])
        w3_sb = sb("w3_sb", [P, H2])
        h1 = sb("h1", [P, H1])
        h1T = sb("h1T", [P, H1 // P, P])
        h2 = sb("h2", [P, H2])
        h2r = sb("h2r", [P, H2])
        y = sb("y", [P, TILES])

        turn_ps = [pb(f"turn_ps{i}", [P, 4, P]) for i in range(2)]
        gram_ps = [pb(f"gram_ps{i}", [P, GB, P]) for i in range(2)]
        h1_ps = pb("h1_ps", [P, H1])
        h2_ps = pb("h2_ps", [P, 2 * H2])

        ids_in = sem("ids_in")
        dense_in = [sem(f"dense_in{t}") for t in range(TILES)]
        hot_id_in = [sem(f"hot_id_in{i}") for i in range(2)]
        raw_in = [sem(f"raw_in{i}") for i in range(2)]
        w1_in = [sem(f"w1_in{p}") for p in range(2)]
        w2_in = sem("w2_in")
        rows_in = sem("rows_in")
        gathered = [[sem(f"gathered{t}_{b}") for b in range(len(turns(t)))] for t in range(TILES)]
        ident_set = sem("ident_set")
        pads_set = sem("pads_set")
        row_set = sem("row_set")
        w1_added = sem("w1_added")
        high_set = sem("high_set")
        w1_high = sem("w1_high")
        w1_low = sem("w1_low")
        z_high = sem("z_high")
        z_low = sem("z_low")
        hot_used = sem("hot_used")
        hot_set = sem("hot_set")
        turned = sem("turned")
        taken = {"act": sem("taken_act"), "dve": sem("taken_dve")}
        grams = sem("grams")
        pulled_dve = sem("pulled_dve")
        pulled_act = sem("pulled_act")
        h1_summed = sem("h1_summed")
        h1_ready = sem("h1_ready")
        h2_summed = sem("h2_summed")
        h2_biased = sem("h2_biased")
        y_ready = sem("y_ready")
        y_stored = sem("y_stored")

        block = ctx.enter_context(nc.Block())

        @block.sync
        def _(sp):
            def load_hot(i):
                if i >= 2:
                    sp.wait_ge(hot_set, (CH + 1) * (i - 1))
                sp.dma_start(hot_id[:, i % 2, :], hot_ids[i, :].partition_broadcast(P)).then_inc(hot_id_in[i % 2], 16)
                if i:
                    sp.dma_start(raw[:, i % 2, :, :], hot_tables[i]).then_inc(raw_in[i % 2], 16)

            def load_dense(t):
                if t >= 2:
                    sp.wait_ge(turned, EVENTS.index(("rows", t - 2, 0)) + 1)
                sp.dma_start(vecs[:, t % 2, 0, :], dense[t * P:(t + 1) * P, :]).then_inc(dense_in[t], 16)

            sp.dma_start(idx[:], ids).then_inc(ids_in, 16)
            load_hot(0)
            load_dense(0)
            load_hot(1)
            load_dense(1)
            load_hot(2)
            load_hot(3)

            def load_w1(p):
                n = min(2, ZT + 1 - 2 * p)
                if p >= 2:
                    sp.wait_ge(w1_low, p - 1)
                sp.dma_start(w1_raw[:, p % 2, 0:n, :], w1[:, 2 * p:2 * p + n, :]).then_inc(w1_in[p % 2], 16)

            load_w1(0)
            load_w1(1)
            sp.dma_start(w2_sb[:], w2).then_inc(w2_in, 16)
            sp.dma_start(b2_sb[:], b2.partition_broadcast(P)).then_inc(rows_in, 16)
            sp.dma_start(w3_sb[:], w3.partition_broadcast(P)).then_inc(rows_in, 16)
            if len(ONEHOT) > 4:
                load_hot(4)
            for p in range(2, W1P):
                load_w1(p)
            for i in range(5, len(ONEHOT)):
                load_hot(i)
            for t in range(2, TILES):
                load_dense(t)
            for t in range(TILES):
                sp.wait_ge(y_ready, t + 1)
                sp.dma_start(out[t * P:(t + 1) * P, :], y[:, t:t + 1]).then_inc(y_stored, 16)
            sp.wait_ge(y_stored, 16 * TILES)

        @block.gpsimd
        def _(pool):
            pool.iota(row_i[:], pattern=[[1, CH]], base=0, channel_multiplier=CH).then_inc(row_set, 1)
            pool.memset(ident[:], 0.0).then_inc(ident_set, 1)
            pool.wait_ge(ident_set, 1)
            pool.affine_select(out=ident[:], in_=ident[:], compare_op=ALU.not_equal, fill=1.0,
                               base=0, pattern=[[-1, P]], channel_multiplier=1).then_inc(ident_set, 1)
            pool.wait_ge(ids_in, 16)
            for t in range(TILES):
                for b, slots in enumerate(turns(t)):
                    if t >= 2:
                        pool.wait_ge(turned, EVENTS.index(("rows", t - 2, b)) + 1)
                    for slot in slots:
                        if slot >= 1:
                            f = SLOT_VEC[slot] - 1
                            pool.indirect_dma_start(
                                vecs[:, t % 2, slot, :], None, tables[f],
                                bass.IndirectOffsetOnAxis(ap=idx[:, t, f:f + 1], axis=0),
                            ).then_inc(gathered[t][b], 16)

        def empty(eng, name, copy, n):
            if EMPTIER[n] != name:
                return
            kind, bank = EVENTS[n][0], turn_ps[n % 2]
            eng.wait_ge(turned, n + 1)
            if kind == "onehot":
                table, first = ONEHOT[EVENTS[n][1]]
                ins = copy(XT[:, first:, :, SLOT_OF[table]],
                           bank[:, first:, :])
            elif kind == "rows":
                t, b = EVENTS[n][1:]
                slots = turns(t)[b]
                ins = copy(XT[:, t, :, slots[0]:slots[-1] + 1],
                           bank[:, 0:len(slots), :].rearrange("p f b -> p b f"))
            else:
                ins = copy(h1T[:], bank[:])
            ins.then_inc(taken[name], 1)

        def pull(eng, copy, quads, t, k, done):
            eng.wait_ge(grams, NGB * t + k + 1)
            for j, mq, n in pulls(quads):
                last = copy(
                    Z[32 * mq:32 * mq + 32, 0:n, 4 * GB * k + j:4 * GB * (k + 1):4].rearrange("p m g -> p g m"),
                    gram_ps[k % 2][32 * j:32 * j + 32, :, NCOL * j + mq:NCOL * (j + 1):4])
            last.then_inc(done, 1)

        def samples(k):
            return slice(4 * GB * k, 4 * GB * (k + 1))

        @block.vector
        def _(dve):
            copy = nc.vector.tensor_copy
            dve.memset(XT[:, :, :, NVEC:SLOTS], 0.0).then_inc(pads_set, 1)
            dve.memset(Z[64:128, MH - 1, :], 0.0).then_inc(pads_set, 1)
            dve.wait_ge(pads_set, 2)
            dve.memset(Z[ONES_ROW:ONES_ROW + 1, MH - 1, :], 1.0).then_inc(pads_set, 1)
            dve.wait_ge(row_set, 1)
            copy(row[:], row_i[:]).then_inc(row_set, 1)
            dve.wait_ge(row_set, 2)

            def split(i):
                slot, first = i % 2, ONEHOT[i][1]

                dve.wait_ge(high_set, i + 1)
                dve.tensor_tensor(low[:, slot], raw[:, slot], high[:, slot].bitcast(F32),
                                  ALU.subtract).then_inc(hot_set, 1)
                dve.wait_ge(hot_id_in[slot], 16 * (i // 2 + 1))
                for c in range(CH):
                    if i >= 1 and c < CH - 1:
                        dve.wait_ge(hot_used, (CH - 1) * (i - 1) + c + 1)
                    elif i >= 1:
                        dve.wait_ge(turned, EVENTS.index(("onehot", i - 1)) + 1)
                    dve.tensor_scalar(hot[:, c, first * P:], hot_id[:, slot, first * P:], row[:, c:c + 1], None,
                                      ALU.is_equal).then_inc(hot_set, 1)

            def w1_piece(p):
                n, raw1 = min(2, ZT + 1 - 2 * p), w1_raw[:, p % 2]
                dve.wait_ge(w1_in[p % 2], 16 * (p // 2 + 1))
                if p == 0:
                    dve.tensor_tensor(raw1[:, 0, :], raw1[:, 0, :], raw1[:, 1, :], ALU.add).then_inc(w1_added, 1)
                    n, to = 1, 0
                else:
                    to = 2 * p - 1
                dve.wait_ge(w1_high, p + 1)
                dve.tensor_tensor(w1l[:, to:to + n, :], raw1[:, 0:n, :], w1h[:, to:to + n, :].bitcast(F32),
                                  ALU.subtract).then_inc(w1_low, 1)

            def lows(t, k):
                dve.wait_ge(z_high, NGB * t + k + 1)
                if k == 0:
                    dve.tensor_tensor(Zl[:, MH, :], XT[:, t, :, 0], Zh[:, MH, :].bitcast(F32), ALU.subtract)
                at = samples(k)
                dve.tensor_tensor(Zl[:, 0:MH, at], Z[:, :, at], Zh[:, 0:MH, at].bitcast(F32),
                                  ALU.subtract).then_inc(z_low, 1)

            def last_layer(t):
                dve.wait_ge(h2_summed, t + 1)
                dve.tensor_tensor(h2[:], h2_ps[:, 0:H2], b2_sb[:], ALU.add).then_inc(h2_biased, 1)
                dve.wait_ge(h2_biased, t + 1)
                nc.vector.scalar_tensor_tensor(h2r[:], h2[:], 0.0, w3_sb[:], ALU.max, ALU.mult,
                                               accum_out=y[:, t:t + 1]).then_inc(y_ready, 1)

            for step in PROGRAM:
                kind, at = step[0], step[1:]
                if kind == "split":
                    split(*at)
                if kind == "gram":
                    pull(dve, copy, (0, 1), *at, pulled_dve)
                if kind == "gram":
                    if at[1] >= 1:
                        lows(at[0], at[1] - 1)
                    if at[1] == NGB - 1:
                        lows(*at)
                if step == ("gram", 0, 0):
                    dve.wait_ge(rows_in, 32)
                if kind == "w1":
                    w1_piece(*at)
                if step in EVENTS:
                    empty(dve, "dve", copy, EVENTS.index(step))
                if kind == "second":
                    last_layer(*at)

        @block.scalar
        def _(act):
            def copy(o, i):
                return nc.scalar.activation(o, i, ACT.Copy)

            act.dma_start(raw[:, 0, :, :], hot_tables[0]).then_inc(raw_in[0], 16)
            for step in PROGRAM:
                kind, at = step[0], step[1:]
                if kind == "split":
                    i = at[0]
                    act.wait_ge(raw_in[i % 2], 16 * (i // 2 + 1))
                    if i >= 2:
                        act.wait_ge(turned, EVENTS.index(("onehot", i - 2)) + 1)
                    copy(high[:, i % 2], raw[:, i % 2]).then_inc(high_set, 1)
                if step == ("gram", 0, 0):
                    act.wait_ge(pads_set, 3)
                if kind == "gram":
                    t, k = at
                    pull(act, copy, (2, 3), t, k, pulled_act)
                    if k == 0:
                        copy(Zh[:, MH, :], XT[:, t, :, 0])
                    act.wait_ge(pulled_act, NGB * t + k + 1)
                    act.wait_ge(pulled_dve, NGB * t + k + 1)
                    copy(Zh[:, 0:MH, samples(k)], Z[:, :, samples(k)]).then_inc(z_high, 1)
                if kind == "w1":
                    p = at[0]
                    n, to = (min(2, ZT + 1 - 2 * p), 2 * p - 1) if p else (1, 0)
                    if p:
                        act.wait_ge(w1_in[p % 2], 16 * (p // 2 + 1))
                    else:
                        act.wait_ge(w1_added, 1)
                    copy(w1h[:, to:to + n, :], w1_raw[:, p % 2, 0:n, :]).then_inc(w1_high, 1)
                if kind == "relu":
                    act.wait_ge(h1_summed, at[0] + 1)
                    nc.scalar.activation(h1[:], h1_ps[:], ACT.Relu).then_inc(h1_ready, 1)
                if step in EVENTS:
                    empty(act, "act", copy, EVENTS.index(step))

        @block.tensor
        def _(pe):
            def taken_out(n):
                name, count = emptied(n)
                pe.wait_ge(taken[name], count)

            def event(step):
                n = EVENTS.index(step)
                if n >= 2:
                    taken_out(n - 2)
                return turn_ps[n % 2]

            def onehot(i):
                bank, slot, first = event(("onehot", i)), i % 2, ONEHOT[i][1]
                for c in range(CH):
                    pe.wait_ge(hot_set, (CH + 1) * i + c + 2)
                    for part in (high, low):
                        mm = nc.tensor.matmul(bank[:, first:, :].rearrange("p t b -> p (t b)"),
                                              part[:, slot, c, :], hot[:, c, first * P:],
                                              start=c == 0 and part is high, stop=c == CH - 1 and part is low)
                    mm.then_inc(hot_used if c < CH - 1 else turned, 1)

            def rows(t, b):
                bank, slots = event(("rows", t, b)), turns(t)[b]
                if b == 0:
                    pe.wait_ge(dense_in[t], 16)
                pe.wait_ge(gathered[t][b], 16 * len([s for s in slots if s >= 1]))
                for i, slot in enumerate(slots):
                    mm = nc.tensor.transpose(bank[:, i, :], vecs[:, t % 2, slot, :], ident[:])
                mm.then_inc(turned, 1)

            def gram(t, k):
                if k == 0:
                    for name in taken:
                        counts = [emptied(n)[1] for n in fills(t) if EMPTIER[n] == name]
                        if counts:
                            pe.wait_ge(taken[name], max(counts))
                if t == k == 0:
                    pe.wait_ge(pads_set, 3)
                if NGB * t + k >= 2:
                    pe.wait_ge(pulled_dve, NGB * t + k - 1)
                    pe.wait_ge(pulled_act, NGB * t + k - 1)
                for g in range(GB):
                    s = QUADS * (GB * k + g)
                    mm = nc.tensor.matmul(gram_ps[k % 2][:, g, 0:QUADS * NCOL],
                                          XT[:, t, s:s + QUADS, :].rearrange("p b s -> p (b s)"),
                                          XT[:, t, s:s + QUADS, 1:NVEC], start=True, stop=True)
                mm.then_inc(grams, 1)

            def first(t):
                if t >= 1:
                    pe.wait_ge(h1_ready, t)
                if t == 0:
                    pe.wait_ge(w1_low, 1)
                pe.wait_ge(z_low, NGB * t + 1)
                nc.tensor.matmul(h1_ps[:], Zh[:, MH, :], w1h[:, 0, :], start=True, stop=False)
                nc.tensor.matmul(h1_ps[:], Zh[:, MH, :], w1l[:, 0, :], start=False, stop=False)
                nc.tensor.matmul(h1_ps[:], Zl[:, MH, :], w1h[:, 0, :], start=False, stop=False)
                pe.wait_ge(z_high, NGB * (t + 1))
                for mh in range(MH):
                    if t == 0:
                        pe.wait_ge(w1_low, mh // 2 + 2)
                    nc.tensor.matmul(h1_ps[:], Zh[:, mh, :], w1h[:, 1 + mh, :], start=False, stop=False)
                    nc.tensor.matmul(h1_ps[:], Zh[:, mh, :], w1l[:, 1 + mh, :], start=False, stop=False)
                pe.wait_ge(z_low, NGB * (t + 1))
                for mh in range(MH):
                    mm = nc.tensor.matmul(h1_ps[:], Zl[:, mh, :], w1h[:, 1 + mh, :], start=False, stop=mh == MH - 1)
                mm.then_inc(h1_summed, 1)

            def hidden(t):
                bank = event(("hidden", t))
                pe.wait_ge(h1_ready, t + 1)
                for c in range(H1 // P):
                    mm = nc.tensor.transpose(bank[:, c, :], h1[:, c * P:(c + 1) * P], ident[:])
                mm.then_inc(turned, 1)

            def second(t):
                if t == 0:
                    pe.wait_ge(w2_in, 16)
                else:
                    pe.wait_ge(h2_biased, t)
                taken_out(EVENTS.index(("hidden", t)))
                for c in range(H1 // P):
                    mm = nc.tensor.matmul(h2_ps[:, 0:H2], h1T[:, c, :], w2_sb[:, c, :],
                                          start=c == 0, stop=c == H1 // P - 1)
                mm.then_inc(h2_summed, 1)

            pe.wait_ge(ident_set, 2)
            parts = {"onehot": onehot, "rows": rows, "gram": gram, "first": first, "hidden": hidden, "second": second}
            for step in PROGRAM:
                if step[0] in parts:
                    parts[step[0]](*step[1:])


def w1_rows():
    import numpy as np
    pairs = NVEC * (NVEC - 1) // 2
    bias, zero = D + pairs + D, D + pairs + D + 1
    rows = np.full((P, 2 + MH), zero)
    for n in range(NVEC):
        for m in range(n + 1, NVEC):
            mh, mq = divmod(m - 1, 4)
            a, b = sorted((SLOT_VEC[n], SLOT_VEC[m]))
            rows[32 * mq + n, 2 + mh] = D + a * (2 * NVEC - a - 1) // 2 + b - a - 1
    rows[ONES_ROW, 2 + MH - 1] = bias
    rows[:, 0] = np.arange(D)
    rows[:, 1] = D + pairs + np.arange(D)
    return rows


def kernel(**inputs):
    import numpy as np
    import concourse.bacc as bacc
    from concourse.bass_utils import run_bass_kernel_spmd as run

    inputs = {k: np.asarray(v) for k, v in inputs.items()}
    w1 = np.concatenate([inputs["W_top1"], inputs["b_top1"][None, :], np.zeros((1, H1), np.float32)])[w1_rows()]
    hot = np.stack([np.pad(inputs[f"tbl_{f}"], ((0, P * CH - inputs[f"tbl_{f}"].shape[0]), (0, 0))) for f, _ in ONEHOT])
    arrays = {
        "dense": inputs["r_dense_proj"],
        "ids": inputs["ids"].reshape(TILES, P, NTAB).transpose(1, 0, 2),
        "hot_ids": inputs["ids"][:, [f for f, _ in ONEHOT]].T,
        "hot_tables": hot.reshape(len(ONEHOT), P, CH, D),
        "w1": w1,
        "w2": inputs["W_top2"].reshape(H1 // P, P, H2).transpose(1, 0, 2),
        "b2": inputs["b_top2"],
        "w3": inputs["W_top3"][:, 0],
    }
    arrays |= {f"tbl_{f}": inputs[f"tbl_{f}"] for f in range(NTAB)}
    arrays = {k: np.ascontiguousarray(v) for k, v in arrays.items()}

    nc = bacc.Bacc("TRN2", target_bir_lowering=False, num_devices=1)
    ap = {k: nc.dram_tensor(k, v.shape, mybir.dt.from_np(v.dtype), kind="ExternalInput").ap()
          for k, v in arrays.items()}
    out = nc.dram_tensor("y_out", (BATCH, 1), F32, kind="ExternalOutput").ap()
    dlrm_tower(nc, ap["dense"], ap["ids"], ap["hot_ids"], ap["hot_tables"], [ap[f"tbl_{f}"] for f in range(NTAB)],
               ap["w1"], ap["w2"], ap["b2"], ap["w3"], out)
    return run(nc, [arrays], core_ids=[0]).results[0]["y_out"]
```

```python
import concourse.bass as bass
from concourse import mybir
from contextlib import ExitStack

P = 128
BATCH, D = 512, 128
NTAB = 26
NVEC = NTAB + 1
SLOTS = 32
H1, H2 = 512, 256
HC = H1 // P
TILES = BATCH // P
QUADS = 4
NCOL = NVEC - 1
GROUPS = P // QUADS
GB = 8
NGB = GROUPS // GB
MH = (NCOL + 3) // 4
ONES_ROW = 96
ZT = MH + 1
W1_PIECES = [range(b, min(b + 2, MH)) for b in range(0, MH, 2)] + [range(MH, MH + 2)]
EARLY = 2
WARM = 28
CH = 8
ONEHOT = [(0, 0), (1, 0), (7, 0), (10, 0), (18, 0), (19, 0)]
F32 = mybir.dt.float32
F32R = mybir.dt.float32r
I32 = mybir.dt.int32
ALU = mybir.AluOpType
ACT = mybir.ActivationFunctionType

_HOT = [f for f, _ in ONEHOT]
SLOT_VEC = [0] + [1 + f for f in range(NTAB) if f not in _HOT] + [1 + f for f in reversed(_HOT)]
SLOT_OF = {v - 1: s for s, v in enumerate(SLOT_VEC) if v}


def turns(t):
    n = NVEC - sum(t >= first for _, first in ONEHOT)
    return [range(b, min(b + 4, n)) for b in range(0, n, 4)]


def parts(t):
    return [range(HC)] if t < TILES - 1 else [range(HC // 2), range(HC // 2, HC)]


def program():
    always = [i for i, (_, first) in enumerate(ONEHOT) if first == 0]
    later = [i for i, (_, first) in enumerate(ONEHOT) if first > 0]
    rows = {t: [("rows", t, b) for b in range(len(turns(t)))] for t in range(TILES)}
    hidden = {t: [("hidden", t, q) for q in range(len(parts(t)))] for t in range(TILES)}
    second = {t: [("second", t, q) for q in range(len(parts(t)))] for t in range(TILES)}
    steps = [("split", 0), ("split", 1)]
    for i in always:
        if i == always[-1]:
            steps += rows[0][:EARLY]
            del rows[0][:EARLY]
        steps += [("onehot", i)] + [("split", i + 2)] * (i + 2 in always) + rows[0][:1]
        steps += [("w1_high", i - 2)] * (i >= 2)
        del rows[0][:1]
    last = len(W1_PIECES) - 1
    steps += rows[0] + [("w1_high", p) for p in range(len(always) - 2, last)]
    steps += [("w1_low", p) for p in range(last - 2)]
    for t in range(TILES):
        ahead = rows.get(t + 1, []) + 6 * [None]
        steps += hidden.get(t - 1, []) + [("gram", t, 0), ahead[0], ("gram", t, 1), ahead[1]]
        steps += [("w1_high", last), ("w1_low", last - 2)] * (t == 0)
        steps += [("gram", t, 2)]
        steps += [("w1_low", last - 1), ("w1_low", last)] * (t == 0)
        steps += [("gram", t, 3), ahead[2]] + second.get(t - 1, [])
        steps += [("first", t, q) for q in range(len(parts(t)))] + [("split", i) for i in later if t == 0]
        steps += [("relu", t, q) for q in range(len(parts(t)))]
        steps += [ahead[3]] + [("onehot", i) for i in later if t == 0] + ahead[4:]
    return [s for s in steps if s] + hidden[TILES - 1] + second[TILES - 1]


PROGRAM = program()
EVENTS = [s for s in PROGRAM if s[0] in ("onehot", "rows", "hidden")]
FIRST_GRAM = EVENTS.index([s for s in PROGRAM[:PROGRAM.index(("gram", 0, 0))] if s in EVENTS][-1]) + 1
EMPTIER = ["act" if n < FIRST_GRAM or n % 2 else "dve" for n in range(len(EVENTS))]


def count(step):
    return [s for s in PROGRAM if s[0] == step[0]].index(step) + 1


def emptied(n):
    return EMPTIER[n], EMPTIER[:n + 1].count(EMPTIER[n])


def low_count(i):
    return (CH + 1) * i + (1 if i else CH + 1)


def fills(t):
    return [n for n, s in enumerate(EVENTS)
            if s[0] == "rows" and s[1] == t or s[0] == "onehot" and ONEHOT[s[1]][1] <= t]


def w1_tiles(p):
    return slice(W1_PIECES[p][0], min(W1_PIECES[p][-1] + 1, ZT))


def pulls(quads):
    return [(j, mq, len(range(mq, NCOL, 4))) for j in quads for mq in range(4)]


def dlrm_tower(nc, dense, ids, hot_ids, hot_tables, tables, w1, w2, b2, w3, out):
    ctx = ExitStack()
    with ctx:
        def sb(name, shape, dtype=F32):
            return ctx.enter_context(nc.sbuf_tensor(name, shape, dtype))

        def pb(name, shape):
            return ctx.enter_context(nc.psum_tensor(name, shape, F32))

        def sem(name):
            return ctx.enter_context(nc.semaphore(name))

        idx = sb("idx", [P, TILES, NTAB], I32)
        ident = sb("ident", [P, P])
        vecs = sb("vecs", [P, 2, len(turns(0)) * 4, D])
        XT = sb("XT", [P, TILES, P, SLOTS])
        Z = sb("Z", [P, MH, P])
        Zh = sb("Zh", [P, ZT, P], F32R)
        Zl = sb("Zl", [P, ZT, P], F32R)
        row_i = sb("row_i", [P, CH], I32)
        row = sb("row", [P, CH])
        hot_id = sb("hot_id", [P, 2, BATCH], I32)
        raw = sb("raw", [P, 2, CH, D])
        high = sb("high", [P, 2, CH, D], F32R)
        low = sb("low", [P, 2, CH, D], F32R)
        hot = sb("hot", [P, CH, BATCH], F32R)
        w1_raw = sb("w1_raw", [P, ZT + 1, H1])
        w1h = sb("w1h", [P, ZT, H1], F32R)
        w1l = sb("w1l", [P, ZT, H1], F32R)
        w2_sb = sb("w2_sb", [P, HC, H2])
        b2_sb = sb("b2_sb", [P, H2])
        w3_sb = sb("w3_sb", [P, H2])
        h1 = sb("h1", [P, H1])
        h1T = sb("h1T", [P, HC, P])
        h2 = sb("h2", [P, H2])
        y = sb("y", [P, TILES])

        turn_ps = [pb(f"turn_ps{i}", [P, 4, P]) for i in range(2)]
        gram_ps = [pb(f"gram_ps{i}", [P, GB, P]) for i in range(2)]
        h1_ps = pb("h1_ps", [P, H1])
        h2_ps = pb("h2_ps", [P, 2 * H2])

        ids_in = sem("ids_in")
        dense_in = [sem(f"dense_in{t}") for t in range(TILES)]
        hot_id_in = [sem(f"hot_id_in{i}") for i in range(2)]
        raw_in = [sem(f"raw_in{i}") for i in range(2)]
        w1_in = [sem(f"w1_in{p}") for p in range(len(W1_PIECES))]
        w2_in = sem("w2_in")
        rows_in = sem("rows_in")
        gathered = [[sem(f"gathered{t}_{b}") for b in range(len(turns(t)))] for t in range(TILES)]
        ident_set = sem("ident_set")
        pads_set = sem("pads_set")
        row_set = sem("row_set")
        w1_added = sem("w1_added")
        high_set = sem("high_set")
        w1_high = sem("w1_high")
        w1_low = sem("w1_low")
        z_high = sem("z_high")
        z_low = sem("z_low")
        hot_used = sem("hot_used")
        hot_set = sem("hot_set")
        turned = sem("turned")
        taken = {"act": sem("taken_act"), "dve": sem("taken_dve")}
        grams = sem("grams")
        pulled_dve = sem("pulled_dve")
        pulled_act = sem("pulled_act")
        h1_summed = sem("h1_summed")
        h1_ready = sem("h1_ready")
        h2_summed = sem("h2_summed")
        h2_biased = sem("h2_biased")
        y_ready = sem("y_ready")
        y_stored = sem("y_stored")

        block = ctx.enter_context(nc.Block())

        @block.sync
        def _(sp):
            def load_hot_id(i):
                if i >= 2:
                    sp.wait_ge(hot_set, (CH + 1) * (i - 1))
                sp.dma_start(hot_id[:, i % 2, :], hot_ids[i, :].partition_broadcast(P)).then_inc(hot_id_in[i % 2], 16)

            def load_raw(i):
                if i >= 2:
                    sp.wait_ge(hot_set, low_count(i - 2))
                sp.dma_start(raw[:, i % 2, :, :], hot_tables[i]).then_inc(raw_in[i % 2], 16)

            def load_dense(t):
                if t >= 2:
                    sp.wait_ge(turned, EVENTS.index(("rows", t - 2, 0)) + 1)
                sp.dma_start(vecs[:, t % 2, 0, :], dense[t * P:(t + 1) * P, :]).then_inc(dense_in[t], 16)

            sp.dma_start(idx[:], ids).then_inc(ids_in, 16)
            load_hot_id(0)
            load_raw(1)
            load_hot_id(1)
            load_dense(0)
            load_dense(1)

            def load_w1(p):
                at = slice(W1_PIECES[p][0], W1_PIECES[p][-1] + 1)
                sp.dma_start(w1_raw[:, at, :], w1[:, at, :]).then_inc(w1_in[p], 16)

            for i in range(2, len(ONEHOT)):
                load_raw(i)
                if i - 2 < len(W1_PIECES):
                    load_w1(i - 2)
                load_hot_id(i)
            for p in range(len(ONEHOT) - 2, len(W1_PIECES)):
                load_w1(p)
            sp.dma_start(w2_sb[:], w2).then_inc(w2_in, 16)
            sp.dma_start(b2_sb[:], b2.partition_broadcast(P)).then_inc(rows_in, 16)
            sp.dma_start(w3_sb[:], w3.partition_broadcast(P)).then_inc(rows_in, 16)
            for t in range(2, TILES):
                load_dense(t)
            for t in range(TILES):
                sp.wait_ge(y_ready, t + 1)
                sp.dma_start(out[t * P:(t + 1) * P, :], y[:, t:t + 1]).then_inc(y_stored, 16)
            sp.wait_ge(y_stored, 16 * TILES)

        @block.gpsimd
        def _(pool):
            pool.iota(row_i[:], pattern=[[1, CH]], base=0, channel_multiplier=CH).then_inc(row_set, 1)
            pool.memset(ident[:], 0.0).then_inc(ident_set, 1)
            pool.wait_ge(ident_set, 1)
            pool.affine_select(out=ident[:], in_=ident[:], compare_op=ALU.not_equal, fill=1.0,
                               base=0, pattern=[[-1, P]], channel_multiplier=1).then_inc(ident_set, 1)
            pool.wait_ge(ids_in, 16)
            for t in range(TILES):
                for b, slots in enumerate(turns(t)):
                    if t >= 2:
                        pool.wait_ge(turned, EVENTS.index(("rows", t - 2, b)) + 1)
                    for slot in slots:
                        if slot >= 1:
                            f = SLOT_VEC[slot] - 1
                            pool.indirect_dma_start(
                                vecs[:, t % 2, slot, :], None, tables[f],
                                bass.IndirectOffsetOnAxis(ap=idx[:, t, f:f + 1], axis=0),
                            ).then_inc(gathered[t][b], 16)

        def empty(eng, name, copy, n):
            if EMPTIER[n] != name:
                return
            kind, bank = EVENTS[n][0], turn_ps[n % 2]
            eng.wait_ge(turned, n + 1)
            if kind == "onehot":
                table, first = ONEHOT[EVENTS[n][1]]
                ins = copy(XT[:, first:, :, SLOT_OF[table]],
                           bank[:, first:, :])
            elif kind == "rows":
                t, b = EVENTS[n][1:]
                slots = turns(t)[b]
                ins = copy(XT[:, t, :, slots[0]:slots[-1] + 1],
                           bank[:, 0:len(slots), :].rearrange("p f b -> p b f"))
            else:
                chunks = parts(EVENTS[n][1])[EVENTS[n][2]]
                ins = copy(h1T[:, chunks[0]:chunks[-1] + 1, :], bank[:, 0:len(chunks), :])
            ins.then_inc(taken[name], 1)

        def pull(eng, copy, quads, t, k, done):
            eng.wait_ge(grams, NGB * t + k + 1)
            for j, mq, n in pulls(quads):
                last = copy(
                    Z[32 * mq:32 * mq + 32, 0:n, 4 * GB * k + j:4 * GB * (k + 1):4].rearrange("p m g -> p g m"),
                    gram_ps[k % 2][32 * j:32 * j + 32, :, NCOL * j + mq:NCOL * (j + 1):4])
            last.then_inc(done, 1)

        def layer1(t, q):
            chunks = parts(t)[q]
            n = P * len(chunks)
            bank = h1_ps[:] if q == 0 else gram_ps[0][:, 0:HC, :].rearrange("p c u -> p (c u)")
            return bank[:, 0:n], slice(P * chunks[0], P * chunks[0] + n)

        def samples(k):
            return slice(4 * GB * k, 4 * GB * (k + 1))

        @block.vector
        def _(dve):
            copy = nc.vector.tensor_copy
            dve.memset(XT[:, :, :, NVEC:SLOTS], 0.0).then_inc(pads_set, 1)
            dve.memset(Z[64:128, MH - 1, :], 0.0).then_inc(pads_set, 1)
            dve.wait_ge(pads_set, 2)
            dve.memset(Z[ONES_ROW:ONES_ROW + 1, MH - 1, :], 1.0).then_inc(pads_set, 1)
            dve.wait_ge(row_set, 1)
            copy(row[:], row_i[:]).then_inc(row_set, 1)
            dve.wait_ge(row_set, 2)

            def split(i):
                slot, first = i % 2, ONEHOT[i][1]

                def low_part():
                    dve.wait_ge(high_set, i + 1)
                    dve.tensor_tensor(low[:, slot], raw[:, slot], high[:, slot].bitcast(F32),
                                      ALU.subtract).then_inc(hot_set, 1)

                if i >= 1:
                    low_part()
                dve.wait_ge(hot_id_in[slot], 16 * (i // 2 + 1))
                for c in range(CH):
                    if i >= 1 and c < CH - 1:
                        dve.wait_ge(hot_used, (CH - 1) * (i - 1) + c + 1)
                    elif i >= 1:
                        dve.wait_ge(turned, EVENTS.index(("onehot", i - 1)) + 1)
                    dve.tensor_scalar(hot[:, c, first * P:], hot_id[:, slot, first * P:], row[:, c:c + 1], None,
                                      ALU.is_equal).then_inc(hot_set, 1)
                if i == 0:
                    low_part()

            def w1_add():
                dve.wait_ge(w1_in[-1], 16)
                dve.tensor_tensor(w1_raw[:, MH, :], w1_raw[:, MH, :], w1_raw[:, MH + 1, :],
                                  ALU.add).then_inc(w1_added, 1)

            def w1_piece(p):
                at = w1_tiles(p)
                dve.wait_ge(w1_high, p + 1)
                dve.tensor_tensor(w1l[:, at, :], w1_raw[:, at, :], w1h[:, at, :].bitcast(F32),
                                  ALU.subtract).then_inc(w1_low, 1)

            def lows(t, k):
                dve.wait_ge(z_high, NGB * t + k + 1)
                if k == 0:
                    dve.tensor_tensor(Zl[:, MH, :], XT[:, t, :, 0], Zh[:, MH, :].bitcast(F32), ALU.subtract)
                at = samples(k)
                dve.tensor_tensor(Zl[:, 0:MH, at], Z[:, :, at], Zh[:, 0:MH, at].bitcast(F32),
                                  ALU.subtract).then_inc(z_low, 1)

            def last_layer(t):
                dve.wait_ge(h2_summed, t + 1)
                dve.tensor_tensor(h2[:], h2_ps[:, 0:H2], b2_sb[:], ALU.add).then_inc(h2_biased, 1)
                dve.wait_ge(h2_biased, t + 1)
                nc.vector.scalar_tensor_tensor(h2[:], h2[:], 0.0, w3_sb[:], ALU.max, ALU.mult,
                                               accum_out=y[:, t:t + 1]).then_inc(y_ready, 1)

            for step in PROGRAM:
                kind, at = step[0], step[1:]
                if kind == "split":
                    split(*at)
                if kind == "gram":
                    pull(dve, copy, (0, 1), *at, pulled_dve)
                if kind == "gram":
                    if at[1] >= 1:
                        lows(at[0], at[1] - 1)
                    if at[1] == NGB - 1:
                        lows(*at)
                if step == ("gram", 0, 0):
                    dve.wait_ge(rows_in, 32)
                if step == ("w1_high", len(W1_PIECES) - 1):
                    w1_add()
                if kind == "w1_low":
                    w1_piece(*at)
                if step in EVENTS:
                    empty(dve, "dve", copy, EVENTS.index(step))
                if kind == "second" and at[1] == len(parts(at[0])) - 1:
                    last_layer(at[0])

        @block.scalar
        def _(act):
            def copy(o, i):
                return nc.scalar.activation(o, i, ACT.Copy)

            act.dma_start(raw[:, 0, :, :], hot_tables[0]).then_inc(raw_in[0], 16)
            for step in PROGRAM:
                kind, at = step[0], step[1:]
                if kind == "split":
                    i = at[0]
                    act.wait_ge(raw_in[i % 2], 16 * (i // 2 + 1))
                    if i >= 2:
                        act.wait_ge(turned, EVENTS.index(("onehot", i - 2)) + 1)
                    copy(high[:, i % 2], raw[:, i % 2]).then_inc(high_set, 1)
                if step == ("gram", 0, 0):
                    act.wait_ge(pads_set, 3)
                if kind == "gram":
                    t, k = at
                    pull(act, copy, (2, 3), t, k, pulled_act)
                    if k == 0:
                        copy(Zh[:, MH, :], XT[:, t, :, 0])
                    act.wait_ge(pulled_act, NGB * t + k + 1)
                    act.wait_ge(pulled_dve, NGB * t + k + 1)
                    copy(Zh[:, 0:MH, samples(k)], Z[:, :, samples(k)]).then_inc(z_high, 1)
                if kind == "w1_high":
                    tiles = w1_tiles(*at)
                    if at[0] == len(W1_PIECES) - 1:
                        act.wait_ge(w1_added, 1)
                    else:
                        act.wait_ge(w1_in[at[0]], 16)
                    copy(w1h[:, tiles, :], w1_raw[:, tiles, :]).then_inc(w1_high, 1)
                if kind == "relu":
                    act.wait_ge(h1_summed, count(("first", *at)))
                    ps, units = layer1(*at)
                    nc.scalar.activation(h1[:, units], ps, ACT.Relu).then_inc(h1_ready, 1)
                if step in EVENTS:
                    empty(act, "act", copy, EVENTS.index(step))

        @block.tensor
        def _(pe):
            def taken_out(n):
                name, count = emptied(n)
                pe.wait_ge(taken[name], count)

            def event(step):
                n = EVENTS.index(step)
                if n >= 2:
                    taken_out(n - 2)
                return turn_ps[n % 2]

            def onehot(i):
                bank, slot, first = event(("onehot", i)), i % 2, ONEHOT[i][1]
                if i == 0:
                    pe.wait_ge(high_set, 1)
                order = [(c, part) for c in range(CH) for part in (high, low)]
                if i == 0:
                    order.sort(key=lambda step: step[1] is low)
                for n, (c, part) in enumerate(order):
                    if part is high:
                        pe.wait_ge(hot_set, (CH + 1) * i + c + (2 if i else 1))
                    elif i == c == 0:
                        pe.wait_ge(hot_set, low_count(0))
                    mm = nc.tensor.matmul(bank[:, first:, :].rearrange("p t b -> p (t b)"),
                                          part[:, slot, c, :], hot[:, c, first * P:],
                                          start=n == 0, stop=n == len(order) - 1)
                    if part is low:
                        mm.then_inc(hot_used if c < CH - 1 else turned, 1)

            def rows(t, b):
                bank, slots = event(("rows", t, b)), turns(t)[b]
                if b == 0:
                    pe.wait_ge(dense_in[t], 16)
                pe.wait_ge(gathered[t][b], 16 * len([s for s in slots if s >= 1]))
                for i, slot in enumerate(slots):
                    mm = nc.tensor.transpose(bank[:, i, :], vecs[:, t % 2, slot, :], ident[:])
                mm.then_inc(turned, 1)

            def gram(t, k):
                if k == 0:
                    for name in taken:
                        counts = [emptied(n)[1] for n in fills(t) if EMPTIER[n] == name]
                        if counts:
                            pe.wait_ge(taken[name], max(counts))
                if t == k == 0:
                    pe.wait_ge(pads_set, 3)
                if NGB * t + k >= 2:
                    pe.wait_ge(pulled_dve, NGB * t + k - 1)
                    pe.wait_ge(pulled_act, NGB * t + k - 1)
                for g in range(GB):
                    s = QUADS * (GB * k + g)
                    mm = nc.tensor.matmul(gram_ps[k % 2][:, g, 0:QUADS * NCOL],
                                          XT[:, t, s:s + QUADS, :].rearrange("p b s -> p (b s)"),
                                          XT[:, t, s:s + QUADS, 1:NVEC], start=True, stop=True)
                mm.then_inc(grams, 1)

            def first(t, q):
                ps, units = layer1(t, q)
                if t >= 1 and q == 0:
                    pe.wait_ge(h1_ready, count(("relu", t, 0)) - 1)
                if t == 0:
                    pe.wait_ge(w1_low, len(W1_PIECES))
                pe.wait_ge(z_low, NGB * t + 1)
                nc.tensor.matmul(ps, Zh[:, MH, :], w1h[:, MH, units], start=True, stop=False)
                nc.tensor.matmul(ps, Zh[:, MH, :], w1l[:, MH, units], start=False, stop=False)
                nc.tensor.matmul(ps, Zl[:, MH, :], w1h[:, MH, units], start=False, stop=False)
                pe.wait_ge(z_high, NGB * (t + 1))
                for mh in range(MH):
                    nc.tensor.matmul(ps, Zh[:, mh, :], w1h[:, mh, units], start=False, stop=False)
                    nc.tensor.matmul(ps, Zh[:, mh, :], w1l[:, mh, units], start=False, stop=False)
                pe.wait_ge(z_low, NGB * (t + 1))
                for mh in range(MH):
                    mm = nc.tensor.matmul(ps, Zl[:, mh, :], w1h[:, mh, units], start=False, stop=mh == MH - 1)
                mm.then_inc(h1_summed, 1)

            def hidden(t, q):
                bank = event(("hidden", t, q))
                pe.wait_ge(h1_ready, count(("relu", t, q)))
                for i, c in enumerate(parts(t)[q]):
                    mm = nc.tensor.transpose(bank[:, i, :], h1[:, c * P:(c + 1) * P], ident[:])
                mm.then_inc(turned, 1)

            def second(t, q):
                if t == 0:
                    pe.wait_ge(w2_in, 16)
                else:
                    pe.wait_ge(h2_biased, t)
                taken_out(EVENTS.index(("hidden", t, q)))
                for c in parts(t)[q]:
                    mm = nc.tensor.matmul(h2_ps[:, 0:H2], h1T[:, c, :], w2_sb[:, c, :], start=c == 0, stop=c == HC - 1)
                if c == HC - 1:
                    mm.then_inc(h2_summed, 1)

            pe.wait_ge(ident_set, 2)
            for _ in range(WARM):
                nc.tensor.transpose(gram_ps[0][:, 0, :], ident[:], ident[:])
            work = {"onehot": onehot, "rows": rows, "gram": gram, "first": first, "hidden": hidden, "second": second}
            for step in PROGRAM:
                if step[0] in work:
                    work[step[0]](*step[1:])


def w1_rows():
    import numpy as np
    pairs = NVEC * (NVEC - 1) // 2
    bias, zero = D + pairs + D, D + pairs + D + 1
    rows = np.full((P, ZT + 1), zero)
    for n in range(NVEC):
        for m in range(n + 1, NVEC):
            mh, mq = divmod(m - 1, 4)
            a, b = sorted((SLOT_VEC[n], SLOT_VEC[m]))
            rows[32 * mq + n, mh] = D + a * (2 * NVEC - a - 1) // 2 + b - a - 1
    rows[ONES_ROW, MH - 1] = bias
    rows[:, MH] = np.arange(D)
    rows[:, MH + 1] = D + pairs + np.arange(D)
    return rows


def kernel(**inputs):
    import numpy as np
    import concourse.bacc as bacc
    from concourse.bass_utils import run_bass_kernel_spmd as run

    inputs = {k: np.asarray(v) for k, v in inputs.items()}
    w1 = np.concatenate([inputs["W_top1"], inputs["b_top1"][None, :], np.zeros((1, H1), np.float32)])[w1_rows()]
    hot = np.stack([np.pad(inputs[f"tbl_{f}"], ((0, P * CH - inputs[f"tbl_{f}"].shape[0]), (0, 0))) for f, _ in ONEHOT])
    arrays = {
        "dense": inputs["r_dense_proj"],
        "ids": inputs["ids"].reshape(TILES, P, NTAB).transpose(1, 0, 2),
        "hot_ids": inputs["ids"][:, [f for f, _ in ONEHOT]].T,
        "hot_tables": hot.reshape(len(ONEHOT), P, CH, D),
        "w1": w1,
        "w2": inputs["W_top2"].reshape(HC, P, H2).transpose(1, 0, 2),
        "b2": inputs["b_top2"],
        "w3": inputs["W_top3"][:, 0],
    }
    arrays |= {f"tbl_{f}": inputs[f"tbl_{f}"] for f in range(NTAB)}
    arrays = {k: np.ascontiguousarray(v) for k, v in arrays.items()}

    nc = bacc.Bacc("TRN2", target_bir_lowering=False, num_devices=1)
    ap = {k: nc.dram_tensor(k, v.shape, mybir.dt.from_np(v.dtype), kind="ExternalInput").ap()
          for k, v in arrays.items()}
    out = nc.dram_tensor("y_out", (BATCH, 1), F32, kind="ExternalOutput").ap()
    dlrm_tower(nc, ap["dense"], ap["ids"], ap["hot_ids"], ap["hot_tables"], [ap[f"tbl_{f}"] for f in range(NTAB)],
               ap["w1"], ap["w2"], ap["b2"], ap["w3"], out)
    return run(nc, [arrays], core_ids=[0]).results[0]["y_out"]
```
